# Optimizing a Trainium2 kernel written in Bass

```python
import numpy as np
import jax
import jax.numpy as jnp

def _softmax(x, axis=-1):
    return jax.nn.softmax(x, axis=axis)

def _gelu(x):
    return jax.nn.gelu(x, approximate=True)

def _silu(x):
    return jax.nn.silu(x)

def _sigmoid(x):
    return jax.nn.sigmoid(x)

def _layernorm(x, axis=-1, eps=1e-05):
    m = jnp.mean(x, axis=axis, keepdims=True)
    v = jnp.var(x, axis=axis, keepdims=True)
    return (x - m) / jnp.sqrt(v + eps)

def _scatter_add(tgt, idx, src, axis=0):
    return tgt.at[idx].add(src)

def _segment_sum(src, seg, n):
    return jax.ops.segment_sum(src, seg, n)
kernel_name = 'mk_flamingo_gated_d1_seqx_r4_b91f9f'

def setup_inputs(seed: int=0):
    np.random.seed(seed)
    _w = jnp.asarray

    def _rec_inputs():
        import jax
        import jax.numpy as jnp
        _rk = jax.random.key(seed)
        x = -0.000125 + 0.9999 * jax.random.normal(jax.random.fold_in(_rk, 1), (4, 512, 512), jnp.float32)
        _lenS = 512 - jax.random.randint(jax.random.fold_in(_rk, 7), (4,), 0, max(1, 512 // 4) + 1, jnp.int32)
        _lenS2 = 512 - jax.random.randint(jax.random.fold_in(_rk, 8), (4,), 0, max(1, 512 // 4) + 1, jnp.int32)
        _ctx_2048P = jax.random.normal(jax.random.fold_in(_rk, 11), (4, 16, 512), jnp.float32)
        _ctx_2048c = jax.random.dirichlet(jax.random.fold_in(_rk, 511), 0.3 * jnp.ones((16,), jnp.float32), (4, 512))
        _ctx_2048t = jnp.einsum('bsk,bkd->bsd', _ctx_2048c, _ctx_2048P)
        _ctx_2048t = _ctx_2048t * jax.lax.rsqrt(jnp.mean(jnp.square(_ctx_2048t)) + 1e-12) * 0.953939
        ctx_2048 = -0.00010331 + 0.999899 * (_ctx_2048t + 0.3 * jax.random.normal(jax.random.fold_in(_rk, 611), (4, 512, 512), jnp.float32))
        _validS = jnp.arange(512)[None, :] < _lenS[:, None]
        _validS2 = jnp.arange(512)[None, :] < _lenS2[:, None]
        _causal = jnp.tril(jnp.ones((512, 512), dtype=bool))
        mask_Bx1xS2_ff0 = jnp.where(jnp.ones((4, 1, 512), dtype=bool), 0.0, -1000000000.0).astype(jnp.float32)
        _g = jax.random.normal(jax.random.fold_in(_rk, 9001), (2, 1), jnp.float32)
        _g = jnp.sign(_g) * jnp.maximum(jnp.abs(_g), 1.0) + (_g == 0) * 1.0
        g_xattn = _g[0]
        g_ffn = _g[1]
        return (x, ctx_2048, mask_Bx1xS2_ff0, g_xattn, g_ffn)
    x, ctx_2048, mask_Bx1xS2_ff0, g_xattn, g_ffn = _rec_inputs()

    def _L0_xattn_setup():
        import jax, jax.numpy as jnp
        import numpy as np
        FP8_E4M3_MAX = 448.0
        EPS = 1e-12

        def _fp8_quant_dequant(x):
            amax = jnp.max(jnp.abs(x))
            scale = FP8_E4M3_MAX / jnp.maximum(amax, EPS)
            q = jnp.clip(x * scale, -FP8_E4M3_MAX, FP8_E4M3_MAX).astype(jnp.float8_e4m3fn)
            return q.astype(jnp.float32) / scale
        key = jax.random.key(seed)
        k1, k2 = jax.random.split(key)
        B, M, K, N = (32, 128, 512, 512)
        inp = jax.random.normal(k1, (B, M, K), dtype=jnp.float32)
        weight = jax.random.normal(k2, (B, K, N), dtype=jnp.float32)
        bias = jnp.zeros((B, 1, N), dtype=jnp.float32)
        return {'input': inp, 'weight': weight, 'bias': bias}
    _L0_xattn_all = _L0_xattn_setup()
    _L0_xattn_in = {k: v for k, v in _L0_xattn_all.items() if k in ()}
    del _L0_xattn_all

    def _L0_ffn_setup():
        import jax, jax.numpy as jnp
        import numpy as np
        B, S, D, K, R = (4, 512, 512, 8, 64)
        key = jax.random.key(seed)
        ks = jax.random.split(key, 7)
        x = jax.random.normal(ks[0], (B, S, D), dtype=jnp.float32)
        U = jax.random.normal(ks[1], (K, D, R), dtype=jnp.float32) * 0.02
        V = jax.random.normal(ks[2], (K, R, D), dtype=jnp.float32) * 0.02
        W1 = jax.random.normal(ks[3], (D, D), dtype=jnp.float32) * 0.02
        b1 = jnp.zeros((D,), dtype=jnp.float32)
        W2 = jax.random.normal(ks[4], (D, K), dtype=jnp.float32) * 0.02
        b2 = jnp.zeros((K,), dtype=jnp.float32)
        return {'x': x, 'U': U, 'V': V, 'W1': W1, 'b1': b1, 'W2': W2, 'b2': b2}
    _L0_ffn_all = _L0_ffn_setup()
    _L0_ffn_in = {k: v for k, v in _L0_ffn_all.items() if k in ('U', 'V', 'W1', 'b1', 'W2', 'b2')}
    del _L0_ffn_all
    return {'x': x, 'ctx_2048': ctx_2048, 'mask_Bx1xS2_ff0': mask_Bx1xS2_ff0, 'g_xattn': g_xattn, 'g_ffn': g_ffn, 'L0_ffn_U': _L0_ffn_in['U'], 'L0_ffn_V': _L0_ffn_in['V'], 'L0_ffn_W1': _L0_ffn_in['W1'], 'L0_ffn_b1': _L0_ffn_in['b1'], 'L0_ffn_W2': _L0_ffn_in['W2'], 'L0_ffn_b2': _L0_ffn_in['b2']}

def reference(x, ctx_2048, mask_Bx1xS2_ff0, g_xattn, g_ffn, L0_ffn_U, L0_ffn_V, L0_ffn_W1, L0_ffn_b1, L0_ffn_W2, L0_ffn_b2):
    import jax
    import jax.numpy as jnp

    def _L0_xattn_ref(input, weight, bias):
        import jax, jax.numpy as jnp
        import numpy as np
        FP8_E4M3_MAX = 448.0
        EPS = 1e-12

        def _fp8_quant_dequant(x):
            amax = jnp.max(jnp.abs(x))
            scale = FP8_E4M3_MAX / jnp.maximum(amax, EPS)
            q = jnp.clip(x * scale, -FP8_E4M3_MAX, FP8_E4M3_MAX).astype(jnp.float8_e4m3fn)
            return q.astype(jnp.float32) / scale
        x_dq = _fp8_quant_dequant(input)
        w_dq = _fp8_quant_dequant(weight)
        out = jnp.einsum('bmk,bkn->bmn', x_dq, w_dq)
        out = out + bias
        return out

    def _L0_ffn_ref(x, U, V, W1, b1, W2, b2):
        import jax, jax.numpy as jnp
        import numpy as np
        B, S, D, K, R = (4, 512, 512, 8, 64)
        h = jax.nn.relu(jnp.einsum('bsd,de->bse', x, W1) + b1)
        alpha = jax.nn.softmax(jnp.einsum('bse,ek->bsk', h, W2) + b2, axis=-1)
        vx = jnp.einsum('krd,bsd->bskr', V, x)
        uvx = jnp.einsum('kdr,bskr->bskd', U, vx)
        out = jnp.einsum('bsk,bskd->bsd', alpha, uvx)
        return out
    x = x + jnp.tanh(g_xattn[0]) * _L0_xattn_ref(_layernorm(x, axis=-1), ctx_2048, mask_Bx1xS2_ff0)
    x = x + jnp.tanh(g_ffn[0]) * _L0_ffn_ref(_layernorm(x, axis=-1), L0_ffn_U, L0_ffn_V, L0_ffn_W1, L0_ffn_b1, L0_ffn_W2, L0_ffn_b2)
    return x

_drawn_inputs = setup_inputs


def setup_inputs(seed=0):
    import zlib

    import numpy as np

    out = dict(_drawn_inputs(seed))
    spreads = {'L0_ffn_b1': (0.0, 0.8), 'L0_ffn_b2': (0.0, 0.8)}
    factors = {'L0_ffn_U': 8.0, 'L0_ffn_V': 8.0, 'L0_ffn_W1': 8.0, 'L0_ffn_W2': 8.0}
    for name, (base, spread) in spreads.items():
        noise = np.random.default_rng([zlib.crc32(name.encode()), seed]).standard_normal(out[name].shape)
        drawn = base * np.exp(spread * noise) if base else spread * noise
        out[name] = jnp.asarray(drawn.astype(out[name].dtype))
    for name, factor in factors.items():
        out[name] = (out[name] * factor).astype(out[name].dtype)
    return out
```

```python
from contextlib import ExitStack

import concourse.bass as bass
from concourse import mybir

F32 = mybir.dt.float32
F16 = mybir.dt.float16
BF16 = mybir.dt.bfloat16
U16 = mybir.dt.uint16
U32 = mybir.dt.uint32
ALU = mybir.AluOpType
ACT = mybir.ActivationFunctionType
AX = mybir.AxisListType
P = 128

FP8_MAX = 448.0
FP8_LEAST = 2.0 ** -6
AMAX_LEAST = 1e-12
LN_EPS = 1e-5
KEEP4 = 2.0 ** 20
EXPONENT = 0x7F800000
EXPONENT16 = 0x7F80
HALF16 = 0x0040
WEIGHT_TOP = 2.0 ** 14
WEIGHT_LEAST = 2.0 ** -100
Z_DOWN = 2.0 ** -9


def gated_block(nc, x_in, ctx_in, mask_in, g_xattn, g_ffn, U_in, V_in, W1_in, b1_in, W2_in, b2_in, out):
    B, S, D = x_in.shape
    K, _, R = U_in.shape
    KR = K * R
    T = S // P
    C = D // P
    E = KR // P
    assert T == C == E == 4 and D == KR == 512 and ctx_in.shape[1] == D
    W = T * D
    HW = W // 2

    with ExitStack() as stack:
        def sb(name, shape, dt=F32):
            return stack.enter_context(nc.sbuf_tensor(name, shape, dt))

        def sem(name):
            return stack.enter_context(nc.semaphore(name))

        x = sb("x", [P, B * T, D])
        xn = sb("xn", [P, B, W])
        cx = sb("cx", [P, B, W])
        xq = sb("xq", [P, T, D], F16)
        cq = sb("cq", [P, C, D], F16)
        xqT = sb("xqT", [P, C, S], F16)
        magic = sb("magic", [P, 2, W], BF16)
        shifted = sb("shifted", [P, 2, HW])
        y = sb("y", [P, T, D])
        yT_hi = sb("yT_hi", [P, C, S], F16)
        yT_lo = sb("yT_lo", [P, C, S], F16)
        hT = sb("hT", [P, C, S])
        z = sb("z", [P, T, KR])
        zT = sb("zT", [P, 2, E, S], F16)
        zT_hi, zT_lo = zT[:, 0], zT[:, 1]
        W1_hi, W1_lo = sb("W1_hi", [P, C, D], F16), sb("W1_lo", [P, C, D], F16)
        VT_hi, VT_lo = sb("VT_hi", [P, C, KR], F16), sb("VT_lo", [P, C, KR], F16)
        UT_hi, UT_lo = sb("UT_hi", [P, E, D], F16), sb("UT_lo", [P, E, D], F16)
        W1_raw, V_raw, VT32 = hT[:, :, :], z[:, :, :], z[:, :, :]
        U_raw = zT[:, :, :, :].rearrange("p a e s -> p (a e s)").bitcast(F32).rearrange("p (c q) -> p c q", q=KR)
        U_raw4 = U_raw.rearrange("p c (k r) -> p c k r", r=R)
        UT32 = xn[:, 0, :].rearrange("p (e d) -> p e d", d=D)
        tmask = sb("tmask", [P, B, D])
        W2 = sb("W2", [P, C, K])
        b1 = sb("b1", [P, C])
        b2 = sb("b2", [P, K])
        gates = sb("gates", [P, 2])
        tgates = sb("tgates", [P, 2])
        ident = sb("ident", [P, P])
        ident16 = sb("ident16", [P, P], F16)
        ones = sb("ones", [3, P])
        minus_half = sb("minus_half", [P, T])
        bn = sb("bn", [P, T, 6])
        mv = sb("mv", [P, B + 1, T, 2])
        ve = sb("ve", [P, B + 1, T])
        root = sb("root", [P, B + 1, T])
        newt = sb("newt", [P, T])
        rstd = sb("rstd", [P, B + 1, T])
        nmr = sb("nmr", [P, B + 1, T])
        wsum = sb("wsum", [P, 3])
        wtop = sb("wtop", [3, 1])
        wdiag = sb("wdiag", [3, 3])
        wpow = sb("wpow", [P, 3])
        wup = sb("wup", [P, 3])
        wdown = sb("wdown", [P, 3])
        amax = sb("amax", [P, 2, B])
        amax2 = sb("amax2", [P, 2])
        atop = sb("atop", [2, 1])
        adiag = sb("adiag", [2, 2])
        aall = sb("aall", [P, 2])
        qrec = sb("qrec", [P, 2])
        qscale = sb("qscale", [P, 2])
        qscale20 = sb("qscale20", [P, 2])
        undo_a = sb("undo_a", [P, 1])
        undo_o = sb("undo_o", [P, 1])
        logit = sb("logit", [P, T, K])
        top = sb("top", [P, T])
        low = sb("low", [P, T, K])
        ex = sb("ex", [P, T, K])
        tot = sb("tot", [P, T])
        rtot = sb("rtot", [P, T])
        alpha = sb("alpha", [P, T, K])

        prod = [stack.enter_context(nc.psum_tensor(f"prod{t}", [P, 512], F32)) for t in range(4)]
        turn = [stack.enter_context(nc.psum_tensor(f"turn{n}", [P, 512], F32)) for n in range(3)]
        logits = stack.enter_context(nc.psum_tensor("logits", [P, 512], F32))
        top_turned, top_all = logits[:, 0:P], logits[:, P:2 * P]

        def turn_x(t):
            return turn[t % 3][:, :].bitcast(F16)[:, 0:D].rearrange("p (c s) -> p c s", s=P)

        def turn_z(t):
            return turn[(T + t) % 3][:, :].rearrange("p (c s) -> p c s", s=P)

        def turn_y(t):
            return turn[(2 * T + t) % 3][:, :].rearrange("p (c s) -> p c s", s=P)

        x_loaded = [sem(f"x_loaded{b}") for b in range(B)]
        ctx_loaded = [sem(f"ctx_loaded{b}") for b in range(B)]
        w_loaded = [sem(f"w_loaded{n}") for n in range(3)]
        small_loaded = sem("small_loaded")
        mask_loaded = sem("mask_loaded")
        out_stored = sem("out_stored")
        consts_ready = sem("consts_ready")
        ones_laid = sem("ones_laid")
        gates_ready = sem("gates_ready")
        w_summed = sem("w_summed")
        wtop_turned = sem("wtop_turned")
        wdiag_ready = sem("wdiag_ready")
        wall_ready = sem("wall_ready")
        wscale_ready = sem("wscale_ready")
        v_turned = sem("v_turned")
        v_out = sem("v_out")
        u_turned = sem("u_turned")
        u_out = sem("u_out")
        w_hi_ready = sem("w_hi_ready")
        w_lo_ready = sem("w_lo_ready")
        var_ready = sem("var_ready")
        root_ready = sem("root_ready")
        ln_ready = sem("ln_ready")
        xn_ready = sem("xn_ready")
        amax_ready = sem("amax_ready")
        atop_turned = sem("atop_turned")
        adiag_ready = sem("adiag_ready")
        aall_ready = sem("aall_ready")
        mask_added = sem("mask_added")
        tmask_ready = sem("tmask_ready")
        qscale_ready = sem("qscale_ready")
        x_scaled = sem("x_scaled")
        ctx_scaled = sem("ctx_scaled")
        xq_ready = sem("xq_ready")
        cq_ready = sem("cq_ready")
        xq_turned = sem("xq_turned")
        xqT_ready = sem("xqT_ready")
        attn_ready = sem("attn_ready")
        x1_ready = sem("x1_ready")
        y_ready = sem("y_ready")
        y_turned = sem("y_turned")
        y_hi_ready = sem("y_hi_ready")
        y_lo_ready = sem("y_lo_ready")
        h_ready = sem("h_ready")
        relu_ready = sem("relu_ready")
        logits_ready = sem("logits_ready")
        low_ready = sem("low_ready")
        ex_ready = sem("ex_ready")
        vy_ready = sem("vy_ready")
        z_ready = sem("z_ready")
        z_turned = sem("z_turned")
        z_hi_ready = sem("z_hi_ready")
        z_lo_ready = sem("z_lo_ready")
        o_ready = sem("o_ready")
        result_ready = sem("result_ready")
        dve_done = sem("dve_done")

        block = stack.enter_context(nc.Block())

        @block.sync
        def _(sp):
            def load_x(b):
                sp.dma_start(x[:, b * T:(b + 1) * T, :],
                             x_in[b].rearrange("(t p) d -> p t d", p=P)).then_inc(x_loaded[b], 16)

            def load_ctx(b):
                sp.dma_start(cx[:, b, :].rearrange("p (c n) -> p c n", n=D),
                             ctx_in[b].rearrange("(c p) n -> p c n", p=P)).then_inc(ctx_loaded[b], 16)

            for b in range(B):
                load_x(b)
                load_ctx(b)
            sp.dma_start(W1_raw, W1_in.rearrange("(c p) e -> p c e", p=P)).then_inc(w_loaded[0], 16)
            sp.dma_start(V_raw, V_in.rearrange("k r d -> (k r) d").rearrange("(e p) d -> p e d", p=P))\
              .then_inc(w_loaded[1], 16)
            sp.dma_start(tmask[:, :, :].rearrange("p b d -> p (b d)"),
                         mask_in.rearrange("b o d -> o (b d)").to_broadcast([P, B * D])).then_inc(mask_loaded, 16)
            for c in range(C):
                sp.dma_start(U_raw4[:, c], U_in[:, c * P:(c + 1) * P, :].rearrange("k p r -> p k r"))\
                  .then_inc(w_loaded[2], 16)

            for b in range(B):
                for t in range(T):
                    sp.wait_ge(result_ready, T * b + t + 1)
                    sp.dma_start(out[b, t * P:(t + 1) * P, :], x[:, b * T + t, :]).then_inc(out_stored, 16)
            sp.wait_ge(out_stored, 16 * B * T)

        @block.gpsimd
        def _(pool):
            for m in (ident, ident16):
                nc.gpsimd.memset(m[:, :], 0.0).then_inc(ones_laid, 1)
            nc.gpsimd.memset(ones[:, :], 1.0)
            nc.gpsimd.memset(minus_half[:, :], -0.5)
            pool.wait_ge(ones_laid, 2)
            for m in (ident, ident16):
                nc.gpsimd.affine_select(out=m[:, :], in_=m[:, :], compare_op=ALU.not_equal, fill=1.0, base=0,
                                        pattern=[[-1, P]], channel_multiplier=1).then_inc(consts_ready, 1)
            pool.wait_ge(consts_ready, 2)

            def inverse_root(n, slot):
                pool.wait_ge(var_ready, n + 1)
                nc.gpsimd.tensor_tensor(root[:, slot, :], ve[:, slot, :], minus_half[:, :], ALU.pow)\
                  .then_inc(root_ready, 1)

            def add_mask(b):
                pool.wait_ge(xn_ready, b + 1)
                for t in range(T):
                    xt = x[:, b * T + t, :]
                    nc.gpsimd.tensor_tensor(xt, xt, tmask[:, b, :], ALU.add).then_inc(mask_added, 1)

            for b in range(B):
                inverse_root(b, b)
            pool.wait_ge(gates_ready, 1)
            pool.wait_ge(mask_loaded, 16)
            nc.gpsimd.tensor_scalar(tmask[:, :, :], tmask[:, :, :], tgates[:, 0:1], 1.0, ALU.mult, ALU.mult)\
              .then_inc(tmask_ready, 1)
            pool.wait_ge(tmask_ready, 1)
            add_mask(0)
            inverse_root(B, B)
            for b in range(1, B):
                add_mask(b)
                inverse_root(B + b, B)

        @block.scalar
        def _(act):
            act.dma_start(gates[:, 0:1], g_xattn.unsqueeze(0).to_broadcast([P, 1])).then_inc(small_loaded, 16)
            act.dma_start(gates[:, 1:2], g_ffn.unsqueeze(0).to_broadcast([P, 1])).then_inc(small_loaded, 16)
            act.dma_start(b2[:, :], b2_in.unsqueeze(0).to_broadcast([P, K])).then_inc(small_loaded, 16)
            act.dma_start(b1[:, :], b1_in.rearrange("(c p) -> p c", p=P),
                          allow_slow_non_contiguous=True).then_inc(small_loaded, 16)
            act.dma_start(W2[:, :, :], W2_in.rearrange("(c p) k -> p c k", p=P)).then_inc(small_loaded, 16)

            def norm_x(b):
                act.wait_ge(ln_ready, b + 1)
                for t in range(T):
                    last = nc.scalar.activation(xn[:, b, t * D:(t + 1) * D], x[:, b * T + t, :], ACT.Identity,
                                                bias=nmr[:, b, t:t + 1], scale=rstd[:, b, t:t + 1])
                last.then_inc(xn_ready, 1)

            def sum_abs(n, raw, junk):
                nc.scalar.activation(junk.bitcast(BF16), raw, ACT.Abs, accum_out=wsum[:, n:n + 1])\
                  .then_inc(w_summed, 1)

            def hi_part(n, hi, raw):
                act.wait_ge(w_summed, n + 1)
                nc.scalar.activation(hi[:, :, :], raw, ACT.Copy, scale=wup[:, n:n + 1]).then_inc(w_hi_ready, 1)

            def scale_half(b, which, h):
                if b:
                    act.wait_ge((xq_ready, cq_ready)[which], 2 * b)
                src = (xn, cx)[which][:, b, h * HW:(h + 1) * HW]
                nc.scalar.activation(magic[:, which, h * HW:(h + 1) * HW], src, ACT.Copy,
                                     scale=qscale20[:, which:which + 1])\
                  .then_inc((x_scaled, ctx_scaled)[which], 1)
                nc.scalar.activation(src, src, ACT.Copy, scale=qscale[:, which:which + 1])\
                  .then_inc((x_scaled, ctx_scaled)[which], 1)

            def turn_out_x(b, tiles=range(T)):
                for t in tiles:
                    act.wait_ge(xq_turned, T * b + t + 1)
                    nc.scalar.activation(xqT[:, :, t * P:(t + 1) * P], turn_x(t), ACT.Copy).then_inc(xqT_ready, 1)

            def norm_x1(b):
                act.wait_ge(ln_ready, B + b + 1)
                for t in range(T + 2):
                    if t < T:
                        nc.scalar.activation(y[:, t, :], x[:, b * T + t, :], ACT.Identity,
                                             bias=nmr[:, B, t:t + 1], scale=rstd[:, B, t:t + 1]).then_inc(y_ready, 1)
                    if t >= 2:
                        act.wait_ge(y_turned, T * b + t - 1)
                        nc.scalar.activation(yT_hi[:, :, (t - 2) * P:(t - 1) * P], turn_y(t - 2), ACT.Copy)\
                          .then_inc(y_hi_ready, 1)

            def relu_h(b, chunks):
                for c in chunks:
                    act.wait_ge(h_ready, C * b + c + 1)
                    nc.scalar.activation(hT[:, c, :], prod[c][:, :], ACT.Relu,
                                         bias=b1[:, c:c + 1], scale=wdown[:, 0:1]).then_inc(relu_ready, 1)

            def exp_low(b):
                act.wait_ge(low_ready, b + 1)
                nc.scalar.activation(ex[:, :, :], low[:, :, :], ACT.Exp).then_inc(ex_ready, 1)

            def hi_z(b):
                for t in range(T):
                    act.wait_ge(z_turned, T * b + t + 1)
                    nc.scalar.activation(zT_hi[:, :, t * P:(t + 1) * P], turn_z(t), ACT.Copy)\
                      .then_inc(z_hi_ready, 1)

            for b in range(B):
                norm_x(b)
            act.wait_ge(small_loaded, 5 * 16)
            nc.scalar.activation(tgates[:, :], gates[:, :], ACT.Tanh).then_inc(gates_ready, 1)
            act.wait_ge(w_loaded[0], 16)
            sum_abs(0, W1_raw, W1_hi[:, :, :])
            act.wait_ge(w_loaded[1], 16)
            sum_abs(1, V_raw, VT_hi[:, :, :])
            act.wait_ge(qscale_ready, 2)
            for which in (1, 0):
                for h in range(2):
                    scale_half(0, which, h)
            act.wait_ge(v_turned, C)
            act.wait_ge(w_summed, 2)
            for c in range(C):
                last = nc.scalar.activation(VT32[:, c, :], prod[c][:, :], ACT.Copy)
            last.then_inc(v_out, 1)
            act.wait_ge(w_loaded[2], 16 * C)
            sum_abs(2, U_raw, UT_hi[:, :, :])
            turn_out_x(0, (0, 1))
            turn_out_x(0, (2, 3))
            act.wait_ge(wscale_ready, 1)
            hi_part(0, W1_hi, W1_raw)
            act.wait_ge(xq_ready, 2)
            for e in range(E):
                act.wait_ge(u_turned, e + 1)
                nc.scalar.activation(UT32[:, e, :], prod[e][:, :], ACT.Copy).then_inc(u_out, 1)
            norm_x1(0)
            act.wait_ge(v_out, 1)
            hi_part(1, VT_hi, VT32)
            act.wait_ge(u_out, E)
            hi_part(2, UT_hi, UT32)
            act.wait_ge(w_lo_ready, 1)
            for b in range(B):
                ahead = b + 1 < B
                if ahead:
                    scale_half(b + 1, 0, 0)
                    scale_half(b + 1, 0, 1)
                relu_h(b, (0, 1))
                if ahead:
                    scale_half(b + 1, 1, 0)
                relu_h(b, (2, 3))
                if ahead:
                    turn_out_x(b + 1)
                exp_low(b)
                if ahead:
                    scale_half(b + 1, 1, 1)
                if b == 0:
                    act.wait_ge(w_lo_ready, 3)
                hi_z(b)
                if ahead:
                    norm_x1(b + 1)

        @block.vector
        def _(dve):
            v = nc.vector
            done = [0]

            def link(ins):
                done[0] += 1
                ins.then_inc(dve_done, 1)

            def join(but=0):
                dve.wait_ge(dve_done, done[0] - but)

            def lo_part(n, lo, raw, hi):
                dve.wait_ge(w_hi_ready, n + 1)
                v.scalar_tensor_tensor(lo[:, :, :], raw, wup[:, n:n + 1], hi[:, :, :], ALU.mult, ALU.subtract)\
                 .then_inc(w_lo_ready, 1)

            def over_partitions(n, top, diag, turned, ready):
                dve.wait_ge(turned, 1)
                link(v.tensor_reduce(top[:, :], top_turned[0:n, :], AX.X, ALU.max))
                join()
                v.tensor_scalar(diag[:, :], ident[0:n, 0:n], top[:, :], None, ALU.mult).then_inc(ready, 1)

            def moments(b, slot):
                for t in range(T):
                    link(v.bn_stats(bn[:, t, :], x[:, b * T + t, :]))
                moments_end(slot)

            def moments_end(slot):
                for t in range(T):
                    join(T - 1)
                    link(v.bn_aggr(mv[:, slot, t, :], bn[:, t, :]))
                join()
                v.tensor_scalar(ve[:, slot, :], mv[:, slot, :, 1], LN_EPS, None, ALU.add).then_inc(var_ready, 1)

            def norms(n, slot):
                dve.wait_ge(root_ready, n + 1)
                dve.wait_ge(var_ready, n + 1)
                link(v.tensor_tensor(newt[:, :], root[:, slot, :], root[:, slot, :], ALU.mult))
                join()
                link(v.tensor_tensor(newt[:, :], newt[:, :], ve[:, slot, :], ALU.mult))
                join()
                link(v.tensor_scalar(newt[:, :], newt[:, :], -0.5, 1.5, ALU.mult, ALU.add))
                join()
                link(v.tensor_tensor(rstd[:, slot, :], root[:, slot, :], newt[:, :], ALU.mult))
                join()
                v.scalar_tensor_tensor(nmr[:, slot, :], mv[:, slot, :, 0], -1.0, rstd[:, slot, :],
                                       ALU.mult, ALU.mult).then_inc(ln_ready, 1)

            def x_max(b):
                dve.wait_ge(xn_ready, b + 1)
                link(v.tensor_reduce(amax[:, 0, b:b + 1], xn[:, b, :], AX.X, ALU.max, apply_absolute_value=True))

            def ctx_max(b):
                dve.wait_ge(ctx_loaded[b], 16)
                link(v.tensor_reduce(amax[:, 1, b:b + 1], cx[:, b, :], AX.X, ALU.max, apply_absolute_value=True))

            def quantise(dst, src, which, halves, scaled, count, ready):
                k = len(halves)
                part = [slice(h * HW, (h + 1) * HW) for h in halves]
                m = [magic[:, which, p] for p in part]
                for i in range(k):
                    dve.wait_ge(scaled, count + 2 * halves[i] + 1)
                    link(v.tensor_scalar(m[i].bitcast(U16), m[i].bitcast(U16), EXPONENT16, HALF16,
                                         ALU.bitwise_and, ALU.bitwise_or))
                least = 1.5 * FP8_LEAST * KEEP4
                for i in range(k):
                    join(k - 1)
                    dve.wait_ge(scaled, count + 2 * halves[i] + 2)
                    link(v.scalar_tensor_tensor(shifted[:, halves[i], :], m[i], least, src[:, part[i]],
                                                ALU.max, ALU.add))
                for i in range(k):
                    join(k - 1)
                    link(v.scalar_tensor_tensor(dst[:, part[i]], m[i], least, shifted[:, halves[i], :],
                                                ALU.max, ALU.subtract))
                for i in range(k):
                    join(k - 1 - i)
                    v.tensor_scalar(dst[:, part[i]], dst[:, part[i]], FP8_MAX, -FP8_MAX, ALU.min, ALU.max)\
                     .then_inc(ready, 1)

            xq2 = xq[:, :, :].rearrange("p t d -> p (t d)")
            cq2 = cq[:, :, :].rearrange("p c n -> p (c n)")

            def quantise_x(b, halves=(0, 1)):
                dve.wait_ge(xq_turned, T * b)
                quantise(xq2, xn[:, b, :], 0, halves, x_scaled, 4 * b, xq_ready)

            def quantise_ctx(b, halves=(0, 1)):
                dve.wait_ge(attn_ready, T * b)
                quantise(cq2, cx[:, b, :], 1, halves, ctx_scaled, 4 * b, cq_ready)

            def add_attn(b, t):
                dve.wait_ge(attn_ready, T * b + t + 1)
                dve.wait_ge(mask_added, T * b + t + 1)
                xt = x[:, b * T + t, :]
                v.scalar_tensor_tensor(xt, prod[t][:, :], undo_a[:, :], xt, ALU.mult, ALU.add)\
                 .then_inc(x1_ready, 1)
                dve.wait_ge(x1_ready, T * b + t + 1)
                link(v.bn_stats(bn[:, t, :], xt))

            def lo_y(b, t):
                dve.wait_ge(y_hi_ready, T * b + t + 1)
                here = slice(t * P, (t + 1) * P)
                v.tensor_tensor(yT_lo[:, :, here], turn_y(t), yT_hi[:, :, here], ALU.subtract)\
                 .then_inc(y_lo_ready, 1)

            def softmax_down(b):
                dve.wait_ge(logits_ready, b + 1)
                lg = logits[:, 0:T * K].rearrange("p (t k) -> p t k", k=K)
                link(v.tensor_tensor(logit[:, :, :], lg, b2[:, :].unsqueeze(1).to_broadcast([P, T, K]), ALU.add))
                join()
                link(v.tensor_reduce(top[:, :], logit[:, :, :], AX.X, ALU.max))
                join()
                v.tensor_tensor(low[:, :, :], logit[:, :, :], top[:, :].unsqueeze(2).to_broadcast([P, T, K]),
                                ALU.subtract).then_inc(low_ready, 1)

            def softmax_up(b):
                dve.wait_ge(ex_ready, b + 1)
                link(v.tensor_reduce(tot[:, :], ex[:, :, :], AX.X, ALU.add))
                join()
                link(v.reciprocal(rtot[:, :], tot[:, :]))
                join()
                link(v.tensor_tensor(alpha[:, :, :], ex[:, :, :], rtot[:, :].unsqueeze(2).to_broadcast([P, T, K]),
                                     ALU.mult))
                join()

            def weigh(b, t):
                dve.wait_ge(vy_ready, T * b + t + 1)
                if t == 0:
                    dve.wait_ge(z_turned, T * b)
                v.scalar_tensor_tensor(z[:, t, :].rearrange("p (k r) -> p k r", r=R),
                                       prod[t][:, :].rearrange("p (k r) -> p k r", r=R), Z_DOWN,
                                       alpha[:, t, :].unsqueeze(2).to_broadcast([P, K, R]),
                                       ALU.mult, ALU.mult).then_inc(z_ready, 1)

            def lo_z(b, t):
                dve.wait_ge(z_hi_ready, T * b + t + 1)
                here = slice(t * P, (t + 1) * P)
                v.tensor_tensor(zT_lo[:, :, here], turn_z(t), zT_hi[:, :, here], ALU.subtract)\
                 .then_inc(z_lo_ready, 1)

            def add_ffn(b, t):
                dve.wait_ge(o_ready, T * b + t + 1)
                xt = x[:, b * T + t, :]
                v.scalar_tensor_tensor(xt, prod[t][:, :], undo_o[:, :], xt, ALU.mult, ALU.add)\
                 .then_inc(result_ready, 1)

            for b in range(B):
                dve.wait_ge(x_loaded[b], 16)
                moments(b, b)
                if b:
                    x_max(b - 1)
                ctx_max(b)
                norms(b, b)
            x_max(B - 1)
            join()
            v.tensor_reduce(amax2[:, :], amax[:, :, :], AX.X, ALU.max).then_inc(amax_ready, 1)
            dve.wait_ge(consts_ready, 2)
            over_partitions(2, atop, adiag, atop_turned, adiag_ready)
            dve.wait_ge(aall_ready, 1)
            link(v.tensor_scalar(aall[:, :], top_all[:, 0:2], AMAX_LEAST, None, ALU.max))
            join()
            link(v.reciprocal(qrec[:, :], aall[:, :]))
            join()
            v.tensor_scalar(qscale20[:, :], qrec[:, :], -FP8_MAX, KEEP4, ALU.mult, ALU.mult).then_inc(qscale_ready, 1)
            v.tensor_scalar(qscale[:, :], qrec[:, :], -FP8_MAX, None, ALU.mult).then_inc(qscale_ready, 1)
            link(v.tensor_scalar(aall[:, :], aall[:, :], 1.0 / FP8_MAX, None, ALU.mult))
            dve.wait_ge(gates_ready, 1)
            join()
            link(v.tensor_tensor(undo_a[:, :], aall[:, 0:1], aall[:, 1:2], ALU.mult))
            join()
            link(v.tensor_tensor(undo_a[:, :], undo_a[:, :], tgates[:, 0:1], ALU.mult))
            quantise_ctx(0, (0,))
            quantise_ctx(0, (1,))
            quantise_x(0, (0,))
            over_partitions(3, wtop, wdiag, wtop_turned, wdiag_ready)
            quantise_x(0, (1,))
            dve.wait_ge(wall_ready, 1)
            link(v.tensor_scalar(wpow[:, :], top_all[:, 0:3], WEIGHT_LEAST, None, ALU.max))
            join()
            link(v.tensor_scalar(wpow[:, :].bitcast(U32), wpow[:, :].bitcast(U32), EXPONENT, None, ALU.bitwise_and))
            join()
            link(v.reciprocal(wup[:, :], wpow[:, :]))
            link(v.tensor_scalar(wdown[:, :], wpow[:, :], 1.0 / WEIGHT_TOP, None, ALU.mult))
            join()
            v.tensor_scalar(wup[:, :], wup[:, :], WEIGHT_TOP, None, ALU.mult).then_inc(wscale_ready, 1)
            add_attn(0, 0)
            add_attn(0, 1)
            add_attn(0, 2)
            add_attn(0, 3)
            moments_end(B)
            link(v.scalar_tensor_tensor(undo_o[:, :], wdown[:, 1:2], 1.0 / Z_DOWN, wdown[:, 2:3], ALU.mult, ALU.mult))
            join()
            link(v.tensor_tensor(undo_o[:, :], undo_o[:, :], tgates[:, 1:2], ALU.mult))
            dve.wait_ge(wscale_ready, 1)
            norms(B, B)
            lo_part(0, W1_lo, W1_raw, W1_hi)
            for t in range(T):
                lo_y(0, t)
            lo_part(1, VT_lo, VT32, VT_hi)
            lo_part(2, UT_lo, UT32, UT_hi)

            for b in range(B):
                ahead = b + 1 < B
                if ahead:
                    quantise_x(b + 1)
                    quantise_ctx(b + 1, (0,))
                softmax_down(b)
                softmax_up(b)
                weigh(b, 0)
                if ahead:
                    quantise_ctx(b + 1, (1,))
                weigh(b, 1)
                lo_z(b, 0)
                weigh(b, 2)
                lo_z(b, 1)
                if ahead:
                    add_attn(b + 1, 0)
                weigh(b, 3)
                lo_z(b, 2)
                if ahead:
                    add_attn(b + 1, 1)
                    add_attn(b + 1, 2)
                lo_z(b, 3)
                if ahead:
                    add_attn(b + 1, 3)
                    moments_end(B)
                    norms(B + b + 1, B)
                add_ffn(b, 0)
                add_ffn(b, 1)
                add_ffn(b, 2)
                if ahead:
                    for t in range(T):
                        lo_y(b + 1, t)
                add_ffn(b, 3)

        @block.tensor
        def _(pe):
            mm, transpose = nc.tensor.matmul, nc.tensor.transpose

            def turn_tile(dst, src, eye):
                for c in range(4):
                    last = transpose(dst[:, c, :], src[:, c * P:(c + 1) * P], eye)
                return last

            def three_pass(dst, a_hi, a_lo, m_hi, m_lo, between=()):
                between = iter(between)
                for c in range(4):
                    mm(dst, a_hi(c), m_hi(c), start=(c == 0), stop=False)
                    next(between, None)
                    mm(dst, a_hi(c), m_lo(c), start=False, stop=False)
                    next(between, None)
                    next(between, None)
                    last = mm(dst, a_lo(c), m_hi(c), start=False, stop=(c == 3))
                    next(between, None)
                return last

            def spread(src, n, top, diag, turned, wanted, ready, meanwhile=None):
                transpose(top_turned[0:n, :], src, ident[:, :]).then_inc(turned, 1)
                if meanwhile:
                    meanwhile()
                pe.wait_ge(wanted, 1)
                mm(top_all[:, 0:n], ones[0:n, :], diag[:, :], start=True, stop=True).then_inc(ready, 1)

            pe.wait_ge(consts_ready, 2)
            pe.wait_ge(w_loaded[1], 16)
            for c in range(C):
                for e in range(E):
                    last = transpose(prod[c][:, e * P:(e + 1) * P], V_raw[:, e, c * P:(c + 1) * P], ident[:, :])
                last.then_inc(v_turned, 1)
            pe.wait_ge(amax_ready, 1)
            spread(amax2[:, :], 2, atop, adiag, atop_turned, adiag_ready, aall_ready)

            def turn_xq(b, tiles=range(T)):
                for t in tiles:
                    pe.wait_ge(xq_ready, 2 * b + t // 2 + 1)
                    if t == 3:
                        pe.wait_ge(xqT_ready, T * b + 1)
                    elif b:
                        pe.wait_ge(y_lo_ready, T * (b - 1) + t + 2)
                    turn_tile(turn_x(t), xq[:, t, :], ident16[:, :]).then_inc(xq_turned, 1)

            def attend(b, t):
                if t == 0:
                    pe.wait_ge(cq_ready, 2 * b + 2)
                if b:
                    pe.wait_ge(z_ready, T * (b - 1) + t + 1)
                pe.wait_ge(xqT_ready, T * b + t + 1)
                for c in range(C):
                    last = mm(prod[t][:, :], xqT[:, c, t * P:(t + 1) * P], cq[:, c, :],
                              start=(c == 0), stop=(c == C - 1))
                last.then_inc(attn_ready, 1)

            def turn_y1(b, t):
                pe.wait_ge(y_ready, T * b + t + 1)
                if t == 3:
                    pe.wait_ge(y_lo_ready, T * b + 1)
                elif b:
                    pe.wait_ge(z_lo_ready, T * (b - 1) + t + 2)
                turn_tile(turn_y(t), y[:, t, :], ident[:, :]).then_inc(y_turned, 1)

            def hidden(b):
                pe.wait_ge(y_lo_ready, T * b + T)
                for e in range(C):
                    if b:
                        pe.wait_ge(result_ready, T * (b - 1) + e + 1)
                    cols = slice(e * P, (e + 1) * P)
                    three_pass(prod[e][:, :], lambda c: W1_hi[:, c, cols], lambda c: W1_lo[:, c, cols],
                               lambda c: yT_hi[:, c, :], lambda c: yT_lo[:, c, :]).then_inc(h_ready, 1)

            def v_products(b, t, between=()):
                rows = slice(t * P, (t + 1) * P)
                three_pass(prod[t][:, :], lambda c: yT_hi[:, c, rows], lambda c: yT_lo[:, c, rows],
                           lambda c: VT_hi[:, c, :], lambda c: VT_lo[:, c, :], between).then_inc(vy_ready, 1)

            def logit_products(b):
                for t in range(T):
                    for c in range(C):
                        last = mm(logits[:, t * K:(t + 1) * K], hT[:, c, t * P:(t + 1) * P], W2[:, c, :],
                                  start=(c == 0), stop=(c == C - 1))
                        if (t, c) == (T - 1, C - 1):
                            last.then_inc(logits_ready, 1)
                        if c % 2:
                            yield

            def turn_z1(b, t, ahead):
                pe.wait_ge(z_ready, T * b + t + 1)
                if t == 3:
                    pe.wait_ge(z_lo_ready, T * b + 1)
                elif ahead:
                    pe.wait_ge(xqT_ready, T * (b + 1) + t + 2)
                turn_tile(turn_z(t), z[:, t, :], ident[:, :]).then_inc(z_turned, 1)

            def o_products(b, t, ahead):
                pe.wait_ge(z_lo_ready, T * b + t + 1)
                if ahead:
                    pe.wait_ge(x1_ready, T * (b + 1) + t + 1)
                rows = slice(t * P, (t + 1) * P)
                three_pass(prod[t][:, :], lambda c: zT_hi[:, c, rows], lambda c: zT_lo[:, c, rows],
                           lambda c: UT_hi[:, c, :], lambda c: UT_lo[:, c, :]).then_inc(o_ready, 1)

            pe.wait_ge(v_out, 1)
            pe.wait_ge(w_summed, 3)
            pe.wait_ge(qscale_ready, 1)
            spread(wsum[:, :], 3, wtop, wdiag, wtop_turned, wdiag_ready, wall_ready, lambda: turn_xq(0, (0, 1)))
            attend(0, 0)
            attend(0, 1)
            turn_xq(0, (2, 3))
            attend(0, 2)
            attend(0, 3)
            for e in range(E):
                pe.wait_ge(x1_ready, e + 1)
                for c in range(C):
                    last = transpose(prod[e][:, c * P:(c + 1) * P], U_raw[:, c, e * P:(e + 1) * P], ident[:, :])
                last.then_inc(u_turned, 1)
            for t in range(T):
                turn_y1(0, t)
            pe.wait_ge(w_lo_ready, 1)
            pe.wait_ge(u_out, E)
            hidden(0)
            for b in range(B):
                ahead = b + 1 < B
                if ahead:
                    turn_xq(b + 1)
                if b:
                    pe.wait_ge(low_ready, b)
                else:
                    pe.wait_ge(w_lo_ready, 2)
                pe.wait_ge(relu_ready, C * (b + 1))
                v_products(b, 0, logit_products(b))
                v_products(b, 1)
                turn_z1(b, 0, ahead)
                v_products(b, 2)
                turn_z1(b, 1, ahead)
                if ahead:
                    attend(b + 1, 0)
                v_products(b, 3)
                turn_z1(b, 2, ahead)
                if ahead:
                    attend(b + 1, 1)
                    attend(b + 1, 2)
                turn_z1(b, 3, ahead)
                if ahead:
                    attend(b + 1, 3)
                if not b:
                    pe.wait_ge(w_lo_ready, 3)
                for t in range(3):
                    o_products(b, t, ahead)
                if ahead:
                    for t in range(T):
                        turn_y1(b + 1, t)
                o_products(b, 3, ahead)
                if ahead:
                    hidden(b + 1)


_INS = ["x", "ctx_2048", "mask_Bx1xS2_ff0", "g_xattn", "g_ffn", "L0_ffn_U", "L0_ffn_V", "L0_ffn_W1", "L0_ffn_b1",
        "L0_ffn_W2", "L0_ffn_b2"]


def kernel(**inputs):
    import numpy as np
    import concourse.bacc as bacc
    from concourse.bass_utils import run_bass_kernel_spmd

    nc = bacc.Bacc("TRN2", target_bir_lowering=False, num_devices=1)
    arrays, args = {}, []
    for name in _INS:
        a = np.ascontiguousarray(inputs[name])
        arrays[f"in_{name}"] = a
        args.append(nc.dram_tensor(f"in_{name}", a.shape, mybir.dt.from_np(a.dtype), kind="ExternalInput").ap())
    out = nc.dram_tensor("out", arrays["in_x"].shape, F32, kind="ExternalOutput").ap()
    gated_block(nc, *args, out)
    result = run_bass_kernel_spmd(nc, [arrays], core_ids=[0])
    return result.results[0]["out"]
```

```python
from contextlib import ExitStack

import concourse.bass as bass
from concourse import mybir

F32 = mybir.dt.float32
F16 = mybir.dt.float16
BF16 = mybir.dt.bfloat16
U16 = mybir.dt.uint16
U32 = mybir.dt.uint32
ALU = mybir.AluOpType
ACT = mybir.ActivationFunctionType
AX = mybir.AxisListType
P = 128

FP8_MAX = 448.0
FP8_LEAST = 2.0 ** -6
AMAX_LEAST = 1e-12
LN_EPS = 1e-5
KEEP4 = 2.0 ** 20
EXPONENT = 0x7F800000
EXPONENT16 = 0x7F80
HALF16 = 0x0040
LEAST16 = 1.5 * FP8_LEAST * KEEP4
LINKS = 29
WEIGHT_TOP = 2.0 ** 14
WEIGHT_LEAST = 2.0 ** -100
Z_DOWN = 2.0 ** -9


def gated_block(nc, x_in, ctx_in, mask_in, g_xattn, g_ffn, U_in, V_in, W1_in, b1_in, W2_in, b2_in, out):
    B, S, D = x_in.shape
    K, _, R = U_in.shape
    KR = K * R
    T = S // P
    C = D // P
    E = KR // P
    assert T == C == E == 4 and D == KR == 512 and ctx_in.shape[1] == D
    W = T * D
    HW = W // 2

    with ExitStack() as stack:
        def sb(name, shape, dt=F32):
            return stack.enter_context(nc.sbuf_tensor(name, shape, dt))

        def sem(name):
            return stack.enter_context(nc.semaphore(name))

        x = sb("x", [P, B * T, D])
        xn = sb("xn", [P, B, W])
        cx = sb("cx", [P, B, W])
        xq = sb("xq", [P, T, D], F16)
        cq = sb("cq", [P, C, D], F16)
        xqT = sb("xqT", [P, C, S], F16)
        magic = sb("magic", [P, 2, W], BF16)
        shifted = sb("shifted", [P, 2, HW])
        y = sb("y", [P, T, D])
        yT_hi = sb("yT_hi", [P, C, S], F16)
        yT_lo = sb("yT_lo", [P, C, S], F16)
        hT = sb("hT", [P, C, S])
        z = sb("z", [P, T, KR])
        zT = sb("zT", [P, 2, E, S], F16)
        zT_hi, zT_lo = zT[:, 0], zT[:, 1]
        W1_hi, W1_lo = sb("W1_hi", [P, C, D], F16), sb("W1_lo", [P, C, D], F16)
        VT_hi, VT_lo = sb("VT_hi", [P, C, KR], F16), sb("VT_lo", [P, C, KR], F16)
        UT_hi, UT_lo = sb("UT_hi", [P, E, D], F16), sb("UT_lo", [P, E, D], F16)
        xq2 = xq[:, :, :].rearrange("p t d -> p (t d)")
        cq2 = cq[:, :, :].rearrange("p c n -> p (c n)")
        W1_raw, V_raw, VT32 = hT[:, :, :], z[:, :, :], z[:, :, :]
        U_raw = zT[:, :, :, :].rearrange("p a e s -> p (a e s)").bitcast(F32).rearrange("p (c q) -> p c q", q=KR)
        U_raw4 = U_raw.rearrange("p c (k r) -> p c k r", r=R)
        UT32 = xn[:, 0, :].rearrange("p (e d) -> p e d", d=D)
        tmask = sb("tmask", [P, B, D])
        W2 = sb("W2", [P, C, K])
        b1 = sb("b1", [P, C])
        b2 = sb("b2", [P, K])
        gates = sb("gates", [P, 2])
        tgates = sb("tgates", [P, 2])
        ident = sb("ident", [P, P])
        ident16 = sb("ident16", [P, P], F16)
        ones = sb("ones", [3, P])
        minus_half = sb("minus_half", [P, T])
        bn = sb("bn", [P, T, 6])
        mv = sb("mv", [P, B + 1, T, 2])
        ve = sb("ve", [P, B + 1, T])
        root = sb("root", [P, B + 1, T])
        newt = sb("newt", [P, T])
        rstd = sb("rstd", [P, B + 1, T])
        nmr = sb("nmr", [P, B + 1, T])
        wsum = sb("wsum", [P, 3])
        wtop = sb("wtop", [3, 1])
        wdiag = sb("wdiag", [3, 3])
        wpow = sb("wpow", [P, 3])
        wup = sb("wup", [P, 3])
        wdown = sb("wdown", [P, 3])
        amax = sb("amax", [P, 2, B])
        amax2 = sb("amax2", [P, 2])
        atop = [sb("atop_x", [1, 1]), sb("atop_ctx", [1, 1])]
        aall = sb("aall", [P, 2])
        qrec = sb("qrec", [P, 2])
        qscale = sb("qscale", [P, 2])
        qscale20 = sb("qscale20", [P, 2])
        undo_a = sb("undo_a", [P, 1])
        undo_o = sb("undo_o", [P, 1])
        logit = sb("logit", [P, T, K])
        top = sb("top", [P, T])
        low = sb("low", [P, T, K])
        ex = sb("ex", [P, T, K])
        tot = sb("tot", [P, T])
        rtot = sb("rtot", [P, T])
        alpha = sb("alpha", [P, T, K])

        prod = [stack.enter_context(nc.psum_tensor(f"prod{t}", [P, 512], F32)) for t in range(4)]
        turn = [stack.enter_context(nc.psum_tensor(f"turn{n}", [P, 512], F32)) for n in range(3)]
        logits = stack.enter_context(nc.psum_tensor("logits", [P, 512], F32))
        top_bank = [turn[0], turn[1], logits]
        turned_at, all_at = slice(0, P), slice(P, P + 1)

        def turn_x(t):
            return turn[t % 3][:, :].bitcast(F16)[:, 0:D].rearrange("p (c s) -> p c s", s=P)

        def turn_z(t):
            return turn[(T + t) % 3][:, :].rearrange("p (c s) -> p c s", s=P)

        def turn_y(t):
            return turn[(2 * T + t) % 3][:, :].rearrange("p (c s) -> p c s", s=P)

        def first(b):
            return isinstance(b, int) and b == 0

        x_begun = sem("x_begun")
        x_loaded = [sem(f"x_loaded{b}") for b in range(B)]
        ctx_loaded = [sem(f"ctx_loaded{b}") for b in range(B)]
        w_loaded = [sem(f"w_loaded{n}") for n in range(3)]
        small_loaded = sem("small_loaded")
        mask_begun = sem("mask_begun")
        mask_loaded = sem("mask_loaded")
        out_stored = sem("out_stored")
        consts_ready = sem("consts_ready")
        ones_laid = sem("ones_laid")
        gates_ready = sem("gates_ready")
        w_summed = sem("w_summed")
        wtop_turned = sem("wtop_turned")
        wdiag_ready = sem("wdiag_ready")
        wall_ready = sem("wall_ready")
        wscale_ready = sem("wscale_ready")
        v_turned = sem("v_turned")
        v_out = sem("v_out")
        u_turned = sem("u_turned")
        u_out = sem("u_out")
        w_scaled = sem("w_scaled")
        w_hi_ready = sem("w_hi_ready")
        w_lo_ready = sem("w_lo_ready")
        var_ready = sem("var_ready")
        root_ready = sem("root_ready")
        ln_ready = sem("ln_ready")
        xn_ready = sem("xn_ready")
        amax_ready = [sem("amax_x_ready"), sem("amax_ctx_ready")]
        atop_turned = [sem("atop_x_turned"), sem("atop_ctx_turned")]
        atop_ready = [sem("atop_x_ready"), sem("atop_ctx_ready")]
        aall_ready = [sem("aall_x_ready"), sem("aall_ctx_ready")]
        mask_added = sem("mask_added")
        tmask_ready = sem("tmask_ready")
        qscale_ready = [sem("qscale_x_ready"), sem("qscale_ctx_ready")]
        x_scaled = sem("x_scaled")
        ctx_scaled = sem("ctx_scaled")
        shifted_ready = sem("shifted_ready")
        grid_ready = sem("grid_ready")
        xq_ready = sem("xq_ready")
        cq_ready = sem("cq_ready")
        xq_turned = sem("xq_turned")
        xqT_ready = sem("xqT_ready")
        attn_ready = sem("attn_ready")
        x1_ready = sem("x1_ready")
        y_even_ready = sem("y_even_ready")
        y_odd_ready = sem("y_odd_ready")
        y_turned = sem("y_turned")
        y_hi_ready = sem("y_hi_ready")
        y_lo_ready = sem("y_lo_ready")
        h_ready = sem("h_ready")
        relu_ready = sem("relu_ready")
        logits_ready = sem("logits_ready")
        low_ready = sem("low_ready")
        ex_ready = sem("ex_ready")
        vy_ready = sem("vy_ready")
        z_ready = sem("z_ready")
        z_turned = sem("z_turned")
        z_hi_ready = sem("z_hi_ready")
        z_lo_ready = sem("z_lo_ready")
        o_ready = sem("o_ready")
        result_ready = sem("result_ready")
        held = sem("held")
        dve_done = sem("dve_done")

        block = stack.enter_context(nc.Block())

        @block.sync
        def _(sp):
            def load_x(b):
                sp.dma_start(x[:, b * T:(b + 1) * T, :],
                             x_in[b].rearrange("(t p) d -> p t d", p=P)).then_inc(x_loaded[b], 16)

            def load_ctx(b):
                sp.dma_start(cx[:, b, :].rearrange("p (c n) -> p c n", n=D),
                             ctx_in[b].rearrange("(c p) n -> p c n", p=P)).then_inc(ctx_loaded[b], 16)

            for t in range(0, T, 2):
                sp.dma_start(x[:, t:t + 2, :], x_in[0, t * P:(t + 2) * P, :].rearrange("(t p) d -> p t d", p=P))\
                  .then_inc(x_loaded[0] if t else x_begun, 16)
            for b in range(1, B):
                load_x(b)
                load_ctx(b - 1)
            load_ctx(B - 1)
            sp.dma_start(tmask[:, 0, :], mask_in[0].to_broadcast([P, D])).then_inc(mask_begun, 16)
            sp.dma_start(W1_raw, W1_in.rearrange("(c p) e -> p c e", p=P)).then_inc(w_loaded[0], 16)
            sp.dma_start(V_raw, V_in.rearrange("k r d -> (k r) d").rearrange("(e p) d -> p e d", p=P))\
              .then_inc(w_loaded[1], 16)
            for c in range(C):
                sp.dma_start(U_raw4[:, c], U_in[:, c * P:(c + 1) * P, :].rearrange("k p r -> p k r"))\
                  .then_inc(w_loaded[2], 16)
            sp.dma_start(tmask[:, 1:, :].rearrange("p b d -> p (b d)"),
                         mask_in[1:].rearrange("b o d -> o (b d)").to_broadcast([P, (B - 1) * D]))\
              .then_inc(mask_loaded, 16)

            with sp.Fori(0, B) as b:
                for t in range(T):
                    sp.wait_ge(result_ready, T * b + t + 1)
                    sp.dma_start(out[b, t * P:(t + 1) * P, :], x[:, b * T + t, :]).then_inc(out_stored, 16)
            sp.wait_ge(out_stored, 16 * B * T)

        @block.gpsimd
        def _(pool):
            for m in (ident, ident16):
                nc.gpsimd.memset(m[:, :], 0.0).then_inc(ones_laid, 1)
            nc.gpsimd.memset(ones[:, :], 1.0)
            nc.gpsimd.memset(minus_half[:, :], -0.5)
            pool.wait_ge(ones_laid, 2)
            for m in (ident, ident16):
                nc.gpsimd.affine_select(out=m[:, :], in_=m[:, :], compare_op=ALU.not_equal, fill=1.0, base=0,
                                        pattern=[[-1, P]], channel_multiplier=1).then_inc(consts_ready, 1)
            pool.wait_ge(consts_ready, 2)

            def inverse_root(n, slot):
                pool.wait_ge(var_ready, n + 1)
                nc.gpsimd.tensor_tensor(root[:, slot, :], ve[:, slot, :], minus_half[:, :], ALU.pow)\
                  .then_inc(root_ready, 1)

            def add_mask(b):
                pool.wait_ge(xn_ready, b + 1)
                for t in range(T):
                    xt = x[:, b * T + t, :]
                    nc.gpsimd.tensor_tensor(xt, xt, tmask[:, b, :], ALU.add).then_inc(mask_added, 1)

            def grid(n, part, which, dst):
                pool.wait_ge(shifted_ready, n + 1)
                nc.gpsimd.tensor_tensor(dst[:, part], magic[:, which, part], shifted[:, n % 2, :], ALU.subtract)\
                  .then_inc(grid_ready, 1)

            def lo_part(n, lo, raw, hi):
                pool.wait_ge(w_hi_ready, n + 1)
                nc.gpsimd.tensor_scalar(raw, raw, wup[:, n:n + 1], 1.0, ALU.mult, ALU.mult).then_inc(w_scaled, 1)
                pool.wait_ge(w_scaled, n + 1)
                nc.gpsimd.tensor_tensor(lo[:, :, :], raw, hi[:, :, :], ALU.subtract).then_inc(w_lo_ready, 1)

            def scale_mask(b):
                nc.gpsimd.tensor_scalar(tmask[:, b, :], tmask[:, b, :], tgates[:, 0:1], 1.0, ALU.mult, ALU.mult)\
                  .then_inc(tmask_ready, 1)

            for b in range(B):
                inverse_root(b, b)
            pool.wait_ge(gates_ready, 1)
            pool.wait_ge(mask_begun, 16)
            scale_mask(0)
            pool.wait_ge(tmask_ready, 1)
            add_mask(0)
            halves = [slice(0, HW), slice(HW, W)]
            grid(0, halves[0], 1, cq2)
            grid(1, halves[1], 1, cq2)
            grid(2, halves[0], 0, xq2)
            lo_part(0, W1_lo, W1_raw, W1_hi)
            inverse_root(B, B)
            lo_part(1, VT_lo, VT32, VT_hi)
            lo_part(2, UT_lo, UT32, UT_hi)
            pool.wait_ge(mask_loaded, 16)
            for b in range(1, B):
                scale_mask(b)
            pool.wait_ge(tmask_ready, B)
            with pool.Fori(1, B) as b:
                add_mask(b)
                inverse_root(b + B, B)

        @block.scalar
        def _(act):
            act.dma_start(gates[:, 0:1], g_xattn.unsqueeze(0).to_broadcast([P, 1])).then_inc(small_loaded, 16)
            act.dma_start(gates[:, 1:2], g_ffn.unsqueeze(0).to_broadcast([P, 1])).then_inc(small_loaded, 16)
            act.dma_start(b2[:, :], b2_in.unsqueeze(0).to_broadcast([P, K])).then_inc(small_loaded, 16)
            act.dma_start(b1[:, :], b1_in.rearrange("(c p) -> p c", p=P),
                          allow_slow_non_contiguous=True).then_inc(small_loaded, 16)
            act.dma_start(W2[:, :, :], W2_in.rearrange("(c p) k -> p c k", p=P)).then_inc(small_loaded, 16)

            def norm_x(b):
                act.wait_ge(ln_ready, b + 1)
                for t in range(T):
                    last = nc.scalar.activation(xn[:, b, t * D:(t + 1) * D], x[:, b * T + t, :], ACT.Identity,
                                                bias=nmr[:, b, t:t + 1], scale=rstd[:, b, t:t + 1])
                last.then_inc(xn_ready, 1)

            def sum_abs(n, raw, junk):
                nc.scalar.activation(junk.bitcast(BF16), raw, ACT.Abs, accum_out=wsum[:, n:n + 1])\
                  .then_inc(w_summed, 1)

            def hi_part(n, hi, raw):
                act.wait_ge(w_summed, n + 1)
                nc.scalar.activation(hi[:, :, :], raw, ACT.Copy, scale=wup[:, n:n + 1]).then_inc(w_hi_ready, 1)

            def scale_half(b, which, h):
                if not first(b):
                    act.wait_ge((xq_ready, cq_ready)[which], 2 * b)
                src = (xn, cx)[which][:, b, h * HW:(h + 1) * HW]
                nc.scalar.activation(magic[:, which, h * HW:(h + 1) * HW], src, ACT.Copy,
                                     scale=qscale20[:, which:which + 1])\
                  .then_inc((x_scaled, ctx_scaled)[which], 1)
                nc.scalar.activation(src, src, ACT.Copy, scale=qscale[:, which:which + 1])\
                  .then_inc((x_scaled, ctx_scaled)[which], 1)

            def turn_out_x(b, tiles=range(T)):
                for t in tiles:
                    act.wait_ge(xq_turned, T * b + t + 1)
                    nc.scalar.activation(xqT[:, :, t * P:(t + 1) * P], turn_x(t), ACT.Copy).then_inc(xqT_ready, 1)

            def norm_x1(b):
                act.wait_ge(ln_ready, B + b + 1)
                for t in range(T + 2):
                    if t < T and t % 2 == 0:
                        nc.scalar.activation(y[:, t, :], x[:, b * T + t, :], ACT.Identity,
                                             bias=nmr[:, B, t:t + 1], scale=rstd[:, B, t:t + 1])\
                          .then_inc(y_even_ready, 1)
                    if t >= 2:
                        act.wait_ge(y_turned, T * b + t - 1)
                        nc.scalar.activation(yT_hi[:, :, (t - 2) * P:(t - 1) * P], turn_y(t - 2), ACT.Copy)\
                          .then_inc(y_hi_ready, 1)

            def relu_h(b, chunks):
                for c in chunks:
                    act.wait_ge(h_ready, C * b + c + 1)
                    nc.scalar.activation(hT[:, c, :], prod[c][:, :], ACT.Relu,
                                         bias=b1[:, c:c + 1], scale=wdown[:, 0:1]).then_inc(relu_ready, 1)

            def exp_low(b):
                act.wait_ge(low_ready, b + 1)
                nc.scalar.activation(ex[:, :, :], low[:, :, :], ACT.Exp).then_inc(ex_ready, 1)

            def hi_z(b):
                for t in range(T):
                    act.wait_ge(z_turned, T * b + t + 1)
                    nc.scalar.activation(zT_hi[:, :, t * P:(t + 1) * P], turn_z(t), ACT.Copy)\
                      .then_inc(z_hi_ready, 1)

            norm_x(0)
            norm_x(1)
            act.wait_ge(small_loaded, 5 * 16)
            nc.scalar.activation(tgates[:, :], gates[:, :], ACT.Tanh).then_inc(gates_ready, 1)
            norm_x(2)
            norm_x(3)
            act.wait_ge(w_loaded[0], 16)
            sum_abs(0, W1_raw, W1_hi[:, :, :])
            act.wait_ge(w_loaded[1], 16)
            sum_abs(1, V_raw, VT_hi[:, :, :])
            act.wait_ge(w_loaded[2], 16 * C)
            sum_abs(2, U_raw, UT_hi[:, :, :])
            act.wait_ge(qscale_ready[1], 2)
            scale_half(0, 1, 0)
            scale_half(0, 1, 1)
            act.wait_ge(qscale_ready[0], 2)
            scale_half(0, 0, 0)
            scale_half(0, 0, 1)
            act.wait_ge(v_turned, C)
            act.wait_ge(w_summed, 2)
            for c in range(C):
                last = nc.scalar.activation(VT32[:, c, :], prod[c][:, :], ACT.Copy)
            last.then_inc(v_out, 1)
            act.wait_ge(wscale_ready, 1)
            hi_part(0, W1_hi, W1_raw)
            turn_out_x(0)
            hi_part(1, VT_hi, VT32)
            act.wait_ge(xq_ready, 2)
            for e in range(E):
                act.wait_ge(u_turned, e + 1)
                nc.scalar.activation(UT32[:, e, :], prod[e][:, :], ACT.Copy).then_inc(u_out, 1)
            norm_x1(0)
            act.wait_ge(u_out, E)
            hi_part(2, UT_hi, UT32)
            act.wait_ge(w_lo_ready, 1)

            def batch(b, ahead):
                if ahead:
                    scale_half(b + 1, 0, 0)
                    scale_half(b + 1, 0, 1)
                relu_h(b, (0, 1))
                if ahead:
                    scale_half(b + 1, 1, 0)
                relu_h(b, (2, 3))
                if ahead:
                    turn_out_x(b + 1, (0, 1, 2))
                    scale_half(b + 1, 1, 1)
                    turn_out_x(b + 1, (3,))
                exp_low(b)
                act.wait_ge(w_lo_ready, 3)
                hi_z(b)
                if ahead:
                    norm_x1(b + 1)

            with act.Fori(0, B - 1) as b:
                batch(b, True)
            batch(B - 1, False)

        @block.vector
        def _(dve):
            v = nc.vector
            done = [0, 0]

            def link(ins):
                done[1] += 1
                ins.then_inc(dve_done, 1)

            def join(but=0):
                dve.wait_ge(dve_done, done[0] + (done[1] - but))

            def top_x_or_ctx(which):
                dve.wait_ge(atop_turned[which], 1)
                v.tensor_reduce(atop[which][:, :], top_bank[which][0:1, turned_at], AX.X, ALU.max)\
                 .then_inc(atop_ready[which], 1)

            def scales(which):
                here = slice(which, which + 1)
                dve.wait_ge(aall_ready[which], 1)
                link(v.tensor_scalar(aall[:, here], top_bank[which][:, all_at], AMAX_LEAST, None, ALU.max))
                join()
                link(v.reciprocal(qrec[:, here], aall[:, here]))
                join()
                v.tensor_scalar(qscale20[:, here], qrec[:, here], -FP8_MAX, KEEP4, ALU.mult, ALU.mult)\
                 .then_inc(qscale_ready[which], 1)
                v.tensor_scalar(qscale[:, here], qrec[:, here], -FP8_MAX, None, ALU.mult)\
                 .then_inc(qscale_ready[which], 1)

            def moments(b, slot):
                for t in range(T):
                    if (b, t) == (0, 2):
                        dve.wait_ge(x_loaded[0], 16)
                    link(v.bn_stats(bn[:, t, :], x[:, b * T + t, :]))
                moments_end(slot)

            def hold():
                dve.sem_inc(held, 1)

            def moments_end(slot):
                for t in range(T):
                    join(T - 1)
                    hold()
                    link(v.bn_aggr(mv[:, slot, t, :], bn[:, t, :]))
                join()
                v.tensor_scalar(ve[:, slot, :], mv[:, slot, :, 1], LN_EPS, None, ALU.add).then_inc(var_ready, 1)

            def norms(n, slot):
                dve.wait_ge(root_ready, n + 1)
                dve.wait_ge(var_ready, n + 1)
                link(v.tensor_tensor(newt[:, :], root[:, slot, :], root[:, slot, :], ALU.mult))
                join()
                link(v.tensor_tensor(newt[:, :], newt[:, :], ve[:, slot, :], ALU.mult))
                join()
                link(v.tensor_scalar(newt[:, :], newt[:, :], -0.5, 1.5, ALU.mult, ALU.add))
                join()
                link(v.tensor_tensor(rstd[:, slot, :], root[:, slot, :], newt[:, :], ALU.mult))
                join()
                v.scalar_tensor_tensor(nmr[:, slot, :], mv[:, slot, :, 0], -1.0, rstd[:, slot, :],
                                       ALU.mult, ALU.mult).then_inc(ln_ready, 1)

            def x_max(b):
                dve.wait_ge(xn_ready, b + 1)
                link(v.tensor_reduce(amax[:, 0, b:b + 1], xn[:, b, :], AX.X, ALU.max, apply_absolute_value=True))

            def ctx_max(b):
                dve.wait_ge(ctx_loaded[b], 16)
                link(v.tensor_reduce(amax[:, 1, b:b + 1], cx[:, b, :], AX.X, ALU.max, apply_absolute_value=True))

            def all_max(which):
                join()
                v.tensor_reduce(amax2[:, which:which + 1], amax[:, which, :], AX.X, ALU.max)\
                 .then_inc(amax_ready[which], 1)

            def quantise(dst, src, which, halves, scaled, count, ready, slot=0, meanwhile=None):
                k = len(halves)
                part = [slice(h * HW, (h + 1) * HW) for h in halves]
                m = [magic[:, which, p] for p in part]
                for i in range(k):
                    dve.wait_ge(scaled, count + 2 * halves[i] + 1)
                    link(v.tensor_scalar(m[i].bitcast(U16), m[i].bitcast(U16), EXPONENT16, HALF16,
                                         ALU.bitwise_and, ALU.bitwise_or))
                for i in range(k):
                    join(k - 1)
                    dve.wait_ge(scaled, count + 2 * halves[i] + 2)
                    link(v.scalar_tensor_tensor(shifted[:, slot + i, :], m[i], LEAST16, src[:, part[i]],
                                                ALU.max, ALU.add))
                if meanwhile:
                    meanwhile()
                for i in range(k):
                    join(k - 1)
                    link(v.scalar_tensor_tensor(dst[:, part[i]], m[i], LEAST16, shifted[:, slot + i, :],
                                                ALU.max, ALU.subtract))
                for i in range(k):
                    join(k - 1 - i)
                    v.tensor_scalar(dst[:, part[i]], dst[:, part[i]], FP8_MAX, -FP8_MAX, ALU.min, ALU.max)\
                     .then_inc(ready, 1)

            def begin_grid(n, part, which):
                scaled = (x_scaled, ctx_scaled)[which]
                m = magic[:, which, part]
                at = (0, 2, 0)[n]
                dve.wait_ge(scaled, at + 1)
                link(v.tensor_scalar(m.bitcast(U16), m.bitcast(U16), EXPONENT16, HALF16,
                                     ALU.bitwise_and, ALU.bitwise_or))
                join()
                link(v.tensor_scalar(m, m, LEAST16, None, ALU.max))
                join()
                dve.wait_ge(scaled, at + 2)
                if n >= 2:
                    dve.wait_ge(grid_ready, n - 1)
                v.tensor_tensor(shifted[:, n % 2, :], m, (xn, cx)[which][:, 0, part], ALU.add)\
                 .then_inc(shifted_ready, 1)

            def end_grid(n, part, dst, ready):
                dve.wait_ge(grid_ready, n + 1)
                v.tensor_scalar(dst[:, part], dst[:, part], FP8_MAX, -FP8_MAX, ALU.min, ALU.max).then_inc(ready, 1)

            def quantise_x(b, halves=(0, 1)):
                dve.wait_ge(xq_turned, T * b)
                quantise(xq2, xn[:, b, :], 0, halves, x_scaled, 4 * b, xq_ready)

            def quantise_ctx(b, halves=(0, 1)):
                dve.wait_ge(attn_ready, T * b)
                quantise(cq2, cx[:, b, :], 1, halves, ctx_scaled, 4 * b, cq_ready, halves[0])

            def add_attn(b, t):
                dve.wait_ge(attn_ready, T * b + t + 1)
                dve.wait_ge(mask_added, T * b + t + 1)
                if t:
                    dve.wait_ge(x1_ready, T * b + t)
                xt = x[:, b * T + t, :]
                v.scalar_tensor_tensor(xt, prod[t][:, :], undo_a[:, :], xt, ALU.mult, ALU.add)\
                 .then_inc(x1_ready, 1)
                if t:
                    link(v.bn_stats(bn[:, t - 1, :], x[:, b * T + (t - 1), :]))

            def last_attn_moments(b):
                dve.wait_ge(x1_ready, T * b + T)
                hold()
                link(v.bn_stats(bn[:, T - 1, :], x[:, b * T + (T - 1), :]))

            def odd_y(b):
                dve.wait_ge(ln_ready, B + b + 1)
                for t in range(1, T, 2):
                    v.tensor_scalar(y[:, t, :], x[:, b * T + t, :], rstd[:, B, t:t + 1], nmr[:, B, t:t + 1],
                                    ALU.mult, ALU.add).then_inc(y_odd_ready, 1)

            def lo_y(b, t):
                dve.wait_ge(y_hi_ready, T * b + t + 1)
                here = slice(t * P, (t + 1) * P)
                v.tensor_tensor(yT_lo[:, :, here], turn_y(t), yT_hi[:, :, here], ALU.subtract)\
                 .then_inc(y_lo_ready, 1)

            def softmax_down(b):
                dve.wait_ge(logits_ready, b + 1)
                lg = logits[:, 0:T * K].rearrange("p (t k) -> p t k", k=K)
                link(v.tensor_tensor(logit[:, :, :], lg, b2[:, :].unsqueeze(1).to_broadcast([P, T, K]), ALU.add))
                join()
                link(v.tensor_reduce(top[:, :], logit[:, :, :], AX.X, ALU.max))
                join()
                v.tensor_tensor(low[:, :, :], logit[:, :, :], top[:, :].unsqueeze(2).to_broadcast([P, T, K]),
                                ALU.subtract).then_inc(low_ready, 1)

            def softmax_up(b):
                dve.wait_ge(ex_ready, b + 1)
                link(v.tensor_reduce(tot[:, :], ex[:, :, :], AX.X, ALU.add))
                join()
                link(v.reciprocal(rtot[:, :], tot[:, :]))
                join()
                link(v.tensor_tensor(alpha[:, :, :], ex[:, :, :], rtot[:, :].unsqueeze(2).to_broadcast([P, T, K]),
                                     ALU.mult))
                join()

            def weigh(b, t):
                dve.wait_ge(vy_ready, T * b + t + 1)
                v.scalar_tensor_tensor(z[:, t, :].rearrange("p (k r) -> p k r", r=R),
                                       prod[t][:, :].rearrange("p (k r) -> p k r", r=R), Z_DOWN,
                                       alpha[:, t, :].unsqueeze(2).to_broadcast([P, K, R]),
                                       ALU.mult, ALU.mult).then_inc(z_ready, 1)

            def lo_z(b, t):
                dve.wait_ge(z_hi_ready, T * b + t + 1)
                here = slice(t * P, (t + 1) * P)
                v.tensor_tensor(zT_lo[:, :, here], turn_z(t), zT_hi[:, :, here], ALU.subtract)\
                 .then_inc(z_lo_ready, 1)

            def add_ffn(b, t):
                dve.wait_ge(o_ready, T * b + t + 1)
                xt = x[:, b * T + t, :]
                v.scalar_tensor_tensor(xt, prod[t][:, :], undo_o[:, :], xt, ALU.mult, ALU.add)\
                 .then_inc(result_ready, 1)

            for b in range(B):
                dve.wait_ge(x_loaded[b] if b else x_begun, 16)
                moments(b, b)
                if b:
                    x_max(b - 1)
                norms(b, b)
                if b:
                    ctx_max(b - 1)
            ctx_max(B - 1)
            all_max(1)
            x_max(B - 1)
            all_max(0)
            top_x_or_ctx(1)
            top_x_or_ctx(0)
            scales(1)
            scales(0)
            dve.wait_ge(qscale_ready[0], 2)
            link(v.tensor_scalar(aall[:, :], aall[:, :], 1.0 / FP8_MAX, None, ALU.mult))
            dve.wait_ge(gates_ready, 1)
            join()
            link(v.tensor_tensor(undo_a[:, :], aall[:, 0:1], aall[:, 1:2], ALU.mult))
            join()
            link(v.tensor_tensor(undo_a[:, :], undo_a[:, :], tgates[:, 0:1], ALU.mult))
            halves = [slice(0, HW), slice(HW, W)]
            begin_grid(0, halves[0], 1)
            begin_grid(1, halves[1], 1)
            end_grid(0, halves[0], cq2, cq_ready)
            dve.wait_ge(wtop_turned, 1)
            link(v.tensor_reduce(wtop[:, :], top_bank[2][0:3, turned_at], AX.X, ALU.max))
            dve.wait_ge(consts_ready, 2)
            join()
            v.tensor_scalar(wdiag[:, :], ident[0:3, 0:3], wtop[:, :], None, ALU.mult).then_inc(wdiag_ready, 1)
            begin_grid(2, halves[0], 0)
            end_grid(1, halves[1], cq2, cq_ready)
            dve.wait_ge(wall_ready, 1)
            link(v.tensor_scalar(wpow[:, :], top_bank[2][:, P:P + 3], WEIGHT_LEAST, None, ALU.max))
            join()
            link(v.tensor_scalar(wpow[:, :].bitcast(U32), wpow[:, :].bitcast(U32), EXPONENT, None, ALU.bitwise_and))
            join()
            link(v.reciprocal(wup[:, :], wpow[:, :]))
            link(v.tensor_scalar(wdown[:, :], wpow[:, :], 1.0 / WEIGHT_TOP, None, ALU.mult))
            join()
            v.tensor_scalar(wup[:, :], wup[:, :], WEIGHT_TOP, None, ALU.mult).then_inc(wscale_ready, 1)
            dve.wait_ge(grid_ready, 2)
            quantise(xq2, xn[:, 0, :], 0, (1,), x_scaled, 0, xq_ready, slot=1,
                     meanwhile=lambda: end_grid(2, halves[0], xq2, xq_ready))
            add_attn(0, 0)
            add_attn(0, 1)
            add_attn(0, 2)
            add_attn(0, 3)
            last_attn_moments(0)
            moments_end(B)
            link(v.scalar_tensor_tensor(undo_o[:, :], wdown[:, 1:2], 1.0 / Z_DOWN, wdown[:, 2:3], ALU.mult, ALU.mult))
            join()
            link(v.tensor_tensor(undo_o[:, :], undo_o[:, :], tgates[:, 1:2], ALU.mult))
            dve.wait_ge(wscale_ready, 1)
            norms(B, B)
            odd_y(0)
            for t in range(T):
                lo_y(0, t)

            def batch(b, ahead):
                if ahead:
                    quantise_x(b + 1)
                    quantise_ctx(b + 1, (0,))
                    quantise_ctx(b + 1, (1,))
                softmax_down(b)
                softmax_up(b)
                weigh(b, 0)
                weigh(b, 1)
                lo_z(b, 0)
                weigh(b, 2)
                lo_z(b, 1)
                weigh(b, 3)
                if ahead:
                    add_attn(b + 1, 0)
                lo_z(b, 2)
                if ahead:
                    add_attn(b + 1, 1)
                    add_attn(b + 1, 2)
                lo_z(b, 3)
                if ahead:
                    add_attn(b + 1, 3)
                    last_attn_moments(b + 1)
                    moments_end(B)
                    norms(B + b + 1, B)
                    odd_y(b + 1)
                add_ffn(b, 0)
                add_ffn(b, 1)
                add_ffn(b, 2)
                if ahead:
                    for t in range(T):
                        lo_y(b + 1, t)
                add_ffn(b, 3)

            before = done[1]
            with dve.Fori(0, B - 1) as b:
                done[:] = b * LINKS + before, 0
                batch(b, True)
            assert done[1] == LINKS
            done[:] = (B - 1) * LINKS + before, 0
            batch(B - 1, False)

        @block.tensor
        def _(pe):
            mm, transpose = nc.tensor.matmul, nc.tensor.transpose

            def turn_tile(dst, src, eye):
                for c in range(4):
                    last = transpose(dst[:, c, :], src[:, c * P:(c + 1) * P], eye)
                return last

            def three_pass(dst, a_hi, a_lo, m_hi, m_lo, between=iter(())):
                for c in range(4):
                    mm(dst, a_hi(c), m_hi(c), start=(c == 0), stop=False)
                    next(between, None)
                    mm(dst, a_hi(c), m_lo(c), start=False, stop=False)
                    next(between, None)
                    last = mm(dst, a_lo(c), m_hi(c), start=False, stop=(c == 3))
                    next(between, None)
                return last

            def keep_warm(bank, n):
                for _ in range(n):
                    mm(bank[:, 0:P], ident16[:, :], ident16[:, :], start=True, stop=True)

            def spread_max(which):
                pe.wait_ge(amax_ready[which], 1)
                transpose(top_bank[which][0:1, turned_at], amax2[:, which:which + 1], ident[:, :])\
                    .then_inc(atop_turned[which], 1)

            def spread_max_end(which):
                pe.wait_ge(atop_ready[which], 1)
                mm(top_bank[which][:, all_at], ones[0:1, :], atop[which][:, :], start=True, stop=True)\
                    .then_inc(aall_ready[which], 1)

            pe.wait_ge(consts_ready, 2)
            pe.wait_ge(w_loaded[1], 16)
            for c in range(C):
                for e in range(E):
                    last = transpose(prod[c][:, e * P:(e + 1) * P], V_raw[:, e, c * P:(c + 1) * P], ident[:, :])
                last.then_inc(v_turned, 1)
            spread_max(1)
            spread_max(0)
            spread_max_end(1)
            spread_max_end(0)

            def turn_xq(b, tiles=range(T)):
                for t in tiles:
                    pe.wait_ge(xq_ready, 2 * b + t // 2 + 1)
                    if t == 3:
                        pe.wait_ge(xqT_ready, T * b + 1)
                    elif not first(b):
                        pe.wait_ge(y_lo_ready, T * (b - 1) + t + 2)
                    turn_tile(turn_x(t), xq[:, t, :], ident16[:, :]).then_inc(xq_turned, 1)

            def attend(b, t):
                if t == 0:
                    pe.wait_ge(cq_ready, 2 * b + 2)
                if not first(b):
                    pe.wait_ge(z_ready, T * (b - 1) + t + 1)
                pe.wait_ge(xqT_ready, T * b + t + 1)
                for c in range(C):
                    last = mm(prod[t][:, :], xqT[:, c, t * P:(t + 1) * P], cq[:, c, :],
                              start=(c == 0), stop=(c == C - 1))
                last.then_inc(attn_ready, 1)

            def turn_y1(b, t):
                pe.wait_ge((y_even_ready, y_odd_ready)[t % 2], T // 2 * b + t // 2 + 1)
                if t == 3:
                    pe.wait_ge(y_lo_ready, T * b + 1)
                elif not first(b):
                    pe.wait_ge(z_lo_ready, T * (b - 1) + t + 2)
                turn_tile(turn_y(t), y[:, t, :], ident[:, :]).then_inc(y_turned, 1)

            def hidden(b):
                pe.wait_ge(y_lo_ready, T * b + T)
                for e in range(C):
                    if not first(b):
                        pe.wait_ge(result_ready, T * (b - 1) + e + 1)
                    cols = slice(e * P, (e + 1) * P)
                    three_pass(prod[e][:, :], lambda c: W1_hi[:, c, cols], lambda c: W1_lo[:, c, cols],
                               lambda c: yT_hi[:, c, :], lambda c: yT_lo[:, c, :]).then_inc(h_ready, 1)

            def v_products(b, t, between=iter(())):
                rows = slice(t * P, (t + 1) * P)
                pe.wait_ge(relu_ready, C * b + t + 1)
                three_pass(prod[t][:, :], lambda c: yT_hi[:, c, rows], lambda c: yT_lo[:, c, rows],
                           lambda c: VT_hi[:, c, :], lambda c: VT_lo[:, c, :], between).then_inc(vy_ready, 1)

            def logit_products(b):
                for _ in range(6):
                    yield
                pe.wait_ge(relu_ready, C * (b + 1))
                for t in range(T):
                    for c in range(C):
                        last = mm(logits[:, t * K:(t + 1) * K], hT[:, c, t * P:(t + 1) * P], W2[:, c, :],
                                  start=(c == 0), stop=(c == C - 1))
                        if (t, c) == (T - 1, C - 1):
                            last.then_inc(logits_ready, 1)
                        yield

            def turn_z1(b, t, ahead):
                pe.wait_ge(z_ready, T * b + t + 1)
                if t == 3:
                    pe.wait_ge(z_lo_ready, T * b + 1)
                elif ahead:
                    pe.wait_ge(xqT_ready, T * (b + 1) + t + 2)
                turn_tile(turn_z(t), z[:, t, :], ident[:, :]).then_inc(z_turned, 1)

            def last_turn(b):
                for _ in range(5):
                    yield
                turn_y1(b, 3)

            def o_products(b, t, ahead, between=iter(())):
                pe.wait_ge(z_lo_ready, T * b + t + 1)
                if ahead:
                    pe.wait_ge(x1_ready, T * (b + 1) + t + 1)
                rows = slice(t * P, (t + 1) * P)
                three_pass(prod[t][:, :], lambda c: zT_hi[:, c, rows], lambda c: zT_lo[:, c, rows],
                           lambda c: UT_hi[:, c, :], lambda c: UT_lo[:, c, :], between).then_inc(o_ready, 1)

            pe.wait_ge(w_summed, 3)
            transpose(top_bank[2][0:3, turned_at], wsum[:, :], ident[:, :]).then_inc(wtop_turned, 1)
            pe.wait_ge(wdiag_ready, 1)
            mm(top_bank[2][:, P:P + 3], ones[:, :], wdiag[:, :], start=True, stop=True).then_inc(wall_ready, 1)
            pe.wait_ge(cq_ready, 1)
            keep_warm(turn[2], 24)
            pe.wait_ge(cq_ready, 2)
            keep_warm(turn[2], 28)
            turn_xq(0, (0, 1))
            pe.wait_ge(v_out, 1)
            attend(0, 0)
            turn_xq(0, (2, 3))
            attend(0, 1)
            attend(0, 2)
            attend(0, 3)
            for e in range(E):
                pe.wait_ge(x1_ready, e + 1)
                for c in range(C):
                    last = transpose(prod[e][:, c * P:(c + 1) * P], U_raw[:, c, e * P:(e + 1) * P], ident[:, :])
                last.then_inc(u_turned, 1)
            pe.wait_ge(wscale_ready, 1)
            keep_warm(logits, 60)
            for t in range(T):
                turn_y1(0, t)
                keep_warm(logits, 5 if t < 3 else 24)
            pe.wait_ge(w_lo_ready, 1)
            pe.wait_ge(u_out, E)
            hidden(0)
            def batch(b, ahead):
                if ahead:
                    turn_xq(b + 1, (0, 1, 2))
                pe.wait_ge(w_lo_ready, 2)
                small = logit_products(b)
                v_products(b, 0, small)
                if ahead:
                    turn_xq(b + 1, (3,))
                v_products(b, 1, small)
                v_products(b, 2)
                turn_z1(b, 0, ahead)
                v_products(b, 3)
                turn_z1(b, 1, ahead)
                if ahead:
                    attend(b + 1, 0)
                    attend(b + 1, 1)
                turn_z1(b, 2, ahead)
                if ahead:
                    attend(b + 1, 2)
                pe.wait_ge(w_lo_ready, 3)
                if not ahead:
                    o_products(b, 0, ahead)
                turn_z1(b, 3, ahead)
                if ahead:
                    attend(b + 1, 3)
                    o_products(b, 0, ahead)
                for t in (1, 2):
                    o_products(b, t, ahead)
                if ahead:
                    for t in range(3):
                        turn_y1(b + 1, t)
                o_products(b, 3, ahead, last_turn(b + 1) if ahead else iter(()))
                if ahead:
                    hidden(b + 1)

            with pe.Fori(0, B - 1) as b:
                batch(b, True)
            batch(B - 1, False)


_INS = ["x", "ctx_2048", "mask_Bx1xS2_ff0", "g_xattn", "g_ffn", "L0_ffn_U", "L0_ffn_V", "L0_ffn_W1", "L0_ffn_b1",
        "L0_ffn_W2", "L0_ffn_b2"]


def kernel(**inputs):
    import numpy as np
    import concourse.bacc as bacc
    from concourse.bass_utils import run_bass_kernel_spmd

    nc = bacc.Bacc("TRN2", target_bir_lowering=False, num_devices=1)
    arrays, args = {}, []
    for name in _INS:
        a = np.ascontiguousarray(inputs[name])
        arrays[f"in_{name}"] = a
        args.append(nc.dram_tensor(f"in_{name}", a.shape, mybir.dt.from_np(a.dtype), kind="ExternalInput").ap())
    out = nc.dram_tensor("out", arrays["in_x"].shape, F32, kind="ExternalOutput").ap()
    gated_block(nc, *args, out)
    result = run_bass_kernel_spmd(nc, [arrays], core_ids=[0])
    return result.results[0]["out"]
```
